# Optimizing a Trainium2 kernel written in Bass

```python
import numpy as np
import jax
import jax.numpy as jnp

def _softmax(x, axis=-1):
    return jax.nn.softmax(x, axis=axis)

def _gelu(x):
    return jax.nn.gelu(x, approximate=True)

def _silu(x):
    return jax.nn.silu(x)

def _sigmoid(x):
    return jax.nn.sigmoid(x)

def _layernorm(x, axis=-1, eps=1e-05):
    m = jnp.mean(x, axis=axis, keepdims=True)
    v = jnp.var(x, axis=axis, keepdims=True)
    return (x - m) / jnp.sqrt(v + eps)

def _scatter_add(tgt, idx, src, axis=0):
    return tgt.at[idx].add(src)

def _segment_sum(src, seg, n):
    return jax.ops.segment_sum(src, seg, n)
kernel_name = 'mk_dlrm_tower_d1_rec_r8_851d7a'

def setup_inputs(seed: int=0):
    np.random.seed(seed)
    _w = jnp.asarray

    def _rec_inputs():
        import jax
        import jax.numpy as jnp
        _tk = jax.random.key(seed)
        dense_ctx = jax.random.normal(jax.random.fold_in(_tk, 190), (2048, 16), jnp.float32)
        ids = jnp.stack([jax.random.randint(jax.random.fold_in(_tk, 200 + f), (2048,), 0, v, jnp.int32) for f, v in enumerate([1000, 12500, 1250, 1250, 125000, 12500, 12500, 1000, 125000, 12500, 1000, 1000, 1000, 125000, 1000, 1250, 1250, 12500, 1000, 1250, 1000, 1000, 1250, 12500, 1250, 12500, 12500, 1000, 1250, 1000, 1000, 1000, 1000, 1000, 1000, 1000, 1000, 1000, 1000, 1000])], axis=1)
        tbl_0 = 0.05 * jax.random.normal(jax.random.fold_in(_tk, 500 + 0), (1000, 64), jnp.float32)
        tbl_1 = 0.05 * jax.random.normal(jax.random.fold_in(_tk, 500 + 1), (12500, 64), jnp.float32)
        tbl_2 = 0.05 * jax.random.normal(jax.random.fold_in(_tk, 500 + 2), (1250, 64), jnp.float32)
        tbl_3 = 0.05 * jax.random.normal(jax.random.fold_in(_tk, 500 + 3), (1250, 64), jnp.float32)
        tbl_4 = 0.05 * jax.random.normal(jax.random.fold_in(_tk, 500 + 4), (125000, 64), jnp.float32)
        tbl_5 = 0.05 * jax.random.normal(jax.random.fold_in(_tk, 500 + 5), (12500, 64), jnp.float32)
        tbl_6 = 0.05 * jax.random.normal(jax.random.fold_in(_tk, 500 + 6), (12500, 64), jnp.float32)
        tbl_7 = 0.05 * jax.random.normal(jax.random.fold_in(_tk, 500 + 7), (1000, 64), jnp.float32)
        tbl_8 = 0.05 * jax.random.normal(jax.random.fold_in(_tk, 500 + 8), (125000, 64), jnp.float32)
        tbl_9 = 0.05 * jax.random.normal(jax.random.fold_in(_tk, 500 + 9), (12500, 64), jnp.float32)
        tbl_10 = 0.05 * jax.random.normal(jax.random.fold_in(_tk, 500 + 10), (1000, 64), jnp.float32)
        tbl_11 = 0.05 * jax.random.normal(jax.random.fold_in(_tk, 500 + 11), (1000, 64), jnp.float32)
        tbl_12 = 0.05 * jax.random.normal(jax.random.fold_in(_tk, 500 + 12), (1000, 64), jnp.float32)
        tbl_13 = 0.05 * jax.random.normal(jax.random.fold_in(_tk, 500 + 13), (125000, 64), jnp.float32)
        tbl_14 = 0.05 * jax.random.normal(jax.random.fold_in(_tk, 500 + 14), (1000, 64), jnp.float32)
        tbl_15 = 0.05 * jax.random.normal(jax.random.fold_in(_tk, 500 + 15), (1250, 64), jnp.float32)
        tbl_16 = 0.05 * jax.random.normal(jax.random.fold_in(_tk, 500 + 16), (1250, 64), jnp.float32)
        tbl_17 = 0.05 * jax.random.normal(jax.random.fold_in(_tk, 500 + 17), (12500, 64), jnp.float32)
        tbl_18 = 0.05 * jax.random.normal(jax.random.fold_in(_tk, 500 + 18), (1000, 64), jnp.float32)
        tbl_19 = 0.05 * jax.random.normal(jax.random.fold_in(_tk, 500 + 19), (1250, 64), jnp.float32)
        tbl_20 = 0.05 * jax.random.normal(jax.random.fold_in(_tk, 500 + 20), (1000, 64), jnp.float32)
        tbl_21 = 0.05 * jax.random.normal(jax.random.fold_in(_tk, 500 + 21), (1000, 64), jnp.float32)
        tbl_22 = 0.05 * jax.random.normal(jax.random.fold_in(_tk, 500 + 22), (1250, 64), jnp.float32)
        tbl_23 = 0.05 * jax.random.normal(jax.random.fold_in(_tk, 500 + 23), (12500, 64), jnp.float32)
        tbl_24 = 0.05 * jax.random.normal(jax.random.fold_in(_tk, 500 + 24), (1250, 64), jnp.float32)
        tbl_25 = 0.05 * jax.random.normal(jax.random.fold_in(_tk, 500 + 25), (12500, 64), jnp.float32)
        tbl_26 = 0.05 * jax.random.normal(jax.random.fold_in(_tk, 500 + 26), (12500, 64), jnp.float32)
        tbl_27 = 0.05 * jax.random.normal(jax.random.fold_in(_tk, 500 + 27), (1000, 64), jnp.float32)
        tbl_28 = 0.05 * jax.random.normal(jax.random.fold_in(_tk, 500 + 28), (1250, 64), jnp.float32)
        tbl_29 = 0.05 * jax.random.normal(jax.random.fold_in(_tk, 500 + 29), (1000, 64), jnp.float32)
        tbl_30 = 0.05 * jax.random.normal(jax.random.fold_in(_tk, 500 + 30), (1000, 64), jnp.float32)
        tbl_31 = 0.05 * jax.random.normal(jax.random.fold_in(_tk, 500 + 31), (1000, 64), jnp.float32)
        tbl_32 = 0.05 * jax.random.normal(jax.random.fold_in(_tk, 500 + 32), (1000, 64), jnp.float32)
        tbl_33 = 0.05 * jax.random.normal(jax.random.fold_in(_tk, 500 + 33), (1000, 64), jnp.float32)
        tbl_34 = 0.05 * jax.random.normal(jax.random.fold_in(_tk, 500 + 34), (1000, 64), jnp.float32)
        tbl_35 = 0.05 * jax.random.normal(jax.random.fold_in(_tk, 500 + 35), (1000, 64), jnp.float32)
        tbl_36 = 0.05 * jax.random.normal(jax.random.fold_in(_tk, 500 + 36), (1000, 64), jnp.float32)
        tbl_37 = 0.05 * jax.random.normal(jax.random.fold_in(_tk, 500 + 37), (1000, 64), jnp.float32)
        tbl_38 = 0.05 * jax.random.normal(jax.random.fold_in(_tk, 500 + 38), (1000, 64), jnp.float32)
        tbl_39 = 0.05 * jax.random.normal(jax.random.fold_in(_tk, 500 + 39), (1000, 64), jnp.float32)
        _rk = jax.random.fold_in(_tk, 7)
        W_top1 = 0.0354441 * jax.random.normal(jax.random.fold_in(_tk, 801), (796, 512), jnp.float32)
        W_top2 = 0.0441942 * jax.random.normal(jax.random.fold_in(_tk, 802), (512, 256), jnp.float32)
        W_top3 = 0.0625 * jax.random.normal(jax.random.fold_in(_tk, 803), (256, 1), jnp.float32)
        b_top1 = jnp.zeros((512,), jnp.float32)
        b_top2 = jnp.zeros((256,), jnp.float32)
        return (dense_ctx, ids, tbl_0, tbl_1, tbl_2, tbl_3, tbl_4, tbl_5, tbl_6, tbl_7, tbl_8, tbl_9, tbl_10, tbl_11, tbl_12, tbl_13, tbl_14, tbl_15, tbl_16, tbl_17, tbl_18, tbl_19, tbl_20, tbl_21, tbl_22, tbl_23, tbl_24, tbl_25, tbl_26, tbl_27, tbl_28, tbl_29, tbl_30, tbl_31, tbl_32, tbl_33, tbl_34, tbl_35, tbl_36, tbl_37, tbl_38, tbl_39, W_top1, b_top1, W_top2, b_top2, W_top3)
    dense_ctx, ids, tbl_0, tbl_1, tbl_2, tbl_3, tbl_4, tbl_5, tbl_6, tbl_7, tbl_8, tbl_9, tbl_10, tbl_11, tbl_12, tbl_13, tbl_14, tbl_15, tbl_16, tbl_17, tbl_18, tbl_19, tbl_20, tbl_21, tbl_22, tbl_23, tbl_24, tbl_25, tbl_26, tbl_27, tbl_28, tbl_29, tbl_30, tbl_31, tbl_32, tbl_33, tbl_34, tbl_35, tbl_36, tbl_37, tbl_38, tbl_39, W_top1, b_top1, W_top2, b_top2, W_top3 = _rec_inputs()

    def _L0_rec_setup():
        import jax, jax.numpy as jnp
        import numpy as np
        B, N, E = (1024, 40, 64)
        P = N * (N - 1) // 2

        def _pair_indices(n):
            row, col = ([], [])
            for i in range(n - 1):
                for j in range(i + 1, n):
                    row.append(i)
                    col.append(j)
            return (np.asarray(row), np.asarray(col))
        key = jax.random.key(seed)
        k1, k2 = jax.random.split(key)
        inputs = jax.random.normal(k1, (B, N, E), dtype=jnp.float32)
        std = float(np.sqrt(2.0 / (E + E)))
        param = jax.random.normal(k2, (E, P, E), dtype=jnp.float32) * std
        return {'inputs': inputs, 'param': param}
    _L0_rec_all = _L0_rec_setup()
    _L0_rec_in = {k: v for k, v in _L0_rec_all.items() if k in ('param',)}
    del _L0_rec_all
    return {'dense_ctx': dense_ctx, 'ids': ids, 'tbl_0': tbl_0, 'tbl_1': tbl_1, 'tbl_2': tbl_2, 'tbl_3': tbl_3, 'tbl_4': tbl_4, 'tbl_5': tbl_5, 'tbl_6': tbl_6, 'tbl_7': tbl_7, 'tbl_8': tbl_8, 'tbl_9': tbl_9, 'tbl_10': tbl_10, 'tbl_11': tbl_11, 'tbl_12': tbl_12, 'tbl_13': tbl_13, 'tbl_14': tbl_14, 'tbl_15': tbl_15, 'tbl_16': tbl_16, 'tbl_17': tbl_17, 'tbl_18': tbl_18, 'tbl_19': tbl_19, 'tbl_20': tbl_20, 'tbl_21': tbl_21, 'tbl_22': tbl_22, 'tbl_23': tbl_23, 'tbl_24': tbl_24, 'tbl_25': tbl_25, 'tbl_26': tbl_26, 'tbl_27': tbl_27, 'tbl_28': tbl_28, 'tbl_29': tbl_29, 'tbl_30': tbl_30, 'tbl_31': tbl_31, 'tbl_32': tbl_32, 'tbl_33': tbl_33, 'tbl_34': tbl_34, 'tbl_35': tbl_35, 'tbl_36': tbl_36, 'tbl_37': tbl_37, 'tbl_38': tbl_38, 'tbl_39': tbl_39, 'W_top1': W_top1, 'b_top1': b_top1, 'W_top2': W_top2, 'b_top2': b_top2, 'W_top3': W_top3, 'L0_rec_param': _L0_rec_in['param']}

def reference(dense_ctx, ids, tbl_0, tbl_1, tbl_2, tbl_3, tbl_4, tbl_5, tbl_6, tbl_7, tbl_8, tbl_9, tbl_10, tbl_11, tbl_12, tbl_13, tbl_14, tbl_15, tbl_16, tbl_17, tbl_18, tbl_19, tbl_20, tbl_21, tbl_22, tbl_23, tbl_24, tbl_25, tbl_26, tbl_27, tbl_28, tbl_29, tbl_30, tbl_31, tbl_32, tbl_33, tbl_34, tbl_35, tbl_36, tbl_37, tbl_38, tbl_39, W_top1, b_top1, W_top2, b_top2, W_top3, L0_rec_param):
    import jax
    import jax.numpy as jnp

    def _L0_rec_ref(inputs, param):
        import jax, jax.numpy as jnp
        import numpy as np
        B, N, E = (1024, 40, 64)
        P = N * (N - 1) // 2

        def _pair_indices(n):
            row, col = ([], [])
            for i in range(n - 1):
                for j in range(i + 1, n):
                    row.append(i)
                    col.append(j)
            return (np.asarray(row), np.asarray(col))
        n = inputs.shape[1]
        rowidx, colidx = _pair_indices(n)
        p = inputs[:, rowidx]
        q = inputs[:, colidx]
        out = jnp.einsum('bie,fie,bif->bi', p, param, q)
        return out[:, None, :]
    e = jnp.stack([tbl_0[ids[:, 0]], tbl_1[ids[:, 1]], tbl_2[ids[:, 2]], tbl_3[ids[:, 3]], tbl_4[ids[:, 4]], tbl_5[ids[:, 5]], tbl_6[ids[:, 6]], tbl_7[ids[:, 7]], tbl_8[ids[:, 8]], tbl_9[ids[:, 9]], tbl_10[ids[:, 10]], tbl_11[ids[:, 11]], tbl_12[ids[:, 12]], tbl_13[ids[:, 13]], tbl_14[ids[:, 14]], tbl_15[ids[:, 15]], tbl_16[ids[:, 16]], tbl_17[ids[:, 17]], tbl_18[ids[:, 18]], tbl_19[ids[:, 19]], tbl_20[ids[:, 20]], tbl_21[ids[:, 21]], tbl_22[ids[:, 22]], tbl_23[ids[:, 23]], tbl_24[ids[:, 24]], tbl_25[ids[:, 25]], tbl_26[ids[:, 26]], tbl_27[ids[:, 27]], tbl_28[ids[:, 28]], tbl_29[ids[:, 29]], tbl_30[ids[:, 30]], tbl_31[ids[:, 31]], tbl_32[ids[:, 32]], tbl_33[ids[:, 33]], tbl_34[ids[:, 34]], tbl_35[ids[:, 35]], tbl_36[ids[:, 36]], tbl_37[ids[:, 37]], tbl_38[ids[:, 38]], tbl_39[ids[:, 39]]], axis=1)
    z = _L0_rec_ref(e, L0_rec_param)
    z = z.reshape(z.shape[0], -1)
    h = jnp.concatenate([z, dense_ctx], axis=1)
    h = jnp.maximum(h @ W_top1 + b_top1, 0.0)
    h = jnp.maximum(h @ W_top2 + b_top2, 0.0)
    y = h @ W_top3
    return y

_drawn_inputs = setup_inputs


def setup_inputs(seed=0):
    import zlib

    import numpy as np

    out = dict(_drawn_inputs(seed))
    spreads = {'b_top1': (0.0, 0.1), 'b_top2': (0.0, 0.1)}
    factors = {}
    for name, (base, spread) in spreads.items():
        noise = np.random.default_rng([zlib.crc32(name.encode()), seed]).standard_normal(out[name].shape)
        drawn = base * np.exp(spread * noise) if base else spread * noise
        out[name] = jnp.asarray(drawn.astype(out[name].dtype))
    for name, factor in factors.items():
        out[name] = (out[name] * factor).astype(out[name].dtype)
    return out
```

```python
from contextlib import ExitStack

import concourse.bass as bass
import numpy as np
from concourse import mybir

F32 = mybir.dt.float32
F32R = mybir.dt.float32r
I32 = mybir.dt.int32
ALU = mybir.AluOpType
ACT = mybir.ActivationFunctionType

P = 128
FIELDS = 40
E = 64
B = 2048
CHUNK = 1024
CHUNKS = B // CHUNK
SUB = 512
SUBS = CHUNK // SUB
BT = CHUNK // P
DENSE = 16
H1, H2 = 512, 256

DUOS = FIELDS // 2
TILES = [(c, k) for c in range(1, FIELDS) for k in range((c + 1) // 2)]
NT = len(TILES)
FIRST = {k * k: k for k in range(DUOS)}
QUAD = 4
NQ = NT // QUAD
SLOTS = P // QUAD // 2
NG = -(-NQ // SLOTS)
DENSE_ROW = 2 * (NQ - (NG - 1) * SLOTS)
assert NT == DUOS * DUOS and NQ * QUAD == NT and DENSE_ROW + DENSE <= 32

Y = 3
PROD = 2 * QUAD
STAGE = 4
PREFETCH = 4
DVE_LOW = 36
LOW_AT = 1
GATHERS = 4
RAW = 2
SPLIT = 2

LEAD, SHORT, LATE = 12, 8, 10
AFTER = {max(k * k - 1, (k + 1) * (k + 1) - (LEAD if k > LATE else SHORT)): k + 1 for k in range(1, DUOS - 1)}
ITEMS = [("duo", 0), ("duo", 1)]
for _t in range(NT):
    ITEMS.append(("tile", _t))
    if _t in AFTER:
        ITEMS.append(("duo", AFTER[_t]))
NI = len(ITEMS)
LOW_AFTER = {}
for _a, _k in AFTER.items():
    if _k == 1:
        continue
    _last = _k * _k - 1
    _ends = [t for t in range(_a + 2, _last + 1) if t % QUAD == QUAD - 1]
    if _k <= LATE + 1:
        _places = min(_a + 2, _last), min(_a + 4, _last)
    else:
        _places = (_ends[0], _ends[1]) if len(_ends) > 1 else (_last, _last)
    for _h, _t in enumerate(_places):
        LOW_AFTER.setdefault(_t, []).append((_k, _h))


def duos_at(t):
    return 2 + sum(a <= t for a in AFTER) if t >= 0 else 0


STEPS = [("h1", s, m) for s in range(SUBS) for m in range(H1 // P)]
STEPS += [("h2", s, m) for s in range(SUBS) for m in range(H2 // P)]
STEPS += [("y", s, 0) for s in range(SUBS)]
MLP = len(STEPS)


def pair_index(r, c):
    return r * (2 * FIELDS - 1 - r) // 2 + c - r - 1


def fm_mlp_kernel(nc, dense_t, ids_t, tables, param_q, W1g, b1t, W2t, b2t, W3t, out):
    out_v = out.rearrange("(a n) o -> a (n o)", n=SUB)
    with ExitStack() as ctx:

        def sb(name, shape, dt=F32):
            return ctx.enter_context(nc.sbuf_tensor(name, shape, dt))

        def sem(name):
            return ctx.enter_context(nc.semaphore(name))

        ident = sb("ident", [P, P])
        sel = sb("sel", [P, 62])
        idx = sb("idx", [P, FIELDS, BT], I32)
        stage = sb("stage", [P, STAGE, BT, 2 * E])
        emb_t = sb("emb_t", [P, DUOS, CHUNK])
        cols = sb("cols", [P, 2, 2, CHUNK], F32R)
        raw = sb("raw", [P, RAW, QUAD * P])
        w_hi = sb("w_hi", [P, SPLIT, QUAD * P], F32R)
        w_lo = sb("w_lo", [P, SPLIT, QUAD * P], F32R)
        prod = sb("prod", [P, PROD, CHUNK])
        z = sb("z", [P, NG, CHUNK])
        W1 = sb("W1", [P, NG, H1])
        W3 = sb("W3", [P, H2 // P])
        b1 = sb("b1", [P, H1 // P])
        b2 = sb("b2", [P, H2 // P])
        y_out = sb("y_out", [1, SUBS, SUB])
        h1 = prod[:, 0:4, :].rearrange("p (s a) (b n) -> p s (a b) n", s=SUBS, n=SUB)
        h2 = prod[:, 4:6, :].rearrange("p s (b n) -> p s b n", n=SUB)
        W2 = prod[:, 6, :].rearrange("p (g n) -> p g n", n=H2)

        ring = ctx.enter_context(nc.psum_tensor("ring", [P, Y, CHUNK], F32))
        z_ps = ctx.enter_context(nc.psum_tensor("z_ps", [P, CHUNK], F32))

        consts_loaded = sem("consts_loaded")
        consts_made = sem("consts_made")
        ident_zero = sem("ident_zero")
        sel_zero = sem("sel_zero")
        idx_loaded = sem("idx_loaded")
        gathered = [sem(f"gathered{i}") for i in range(STAGE)]
        pool_waited = sem("pool_waited")
        cols_hi = sem("cols_hi")
        raw_loaded = [sem(f"raw_loaded{i}") for i in range(RAW)]
        hi_ready = sem("hi_ready")
        lo_ready = sem("lo_ready")
        lo_ready_dve = sem("lo_ready_dve")
        item_ready = sem("item_ready")
        tile_done = sem("tile_done")
        duo_saved = sem("duo_saved")
        cols_ready = sem("cols_ready")
        quad_summed = sem("quad_summed")
        z_saved = sem("z_saved")
        dense_loaded = sem("dense_loaded")
        W2_loaded = sem("W2_loaded")
        mlp_ready = sem("mlp_ready")
        mlp_used = sem("mlp_used")
        stored = sem("stored")

        block = ctx.enter_context(nc.Block())

        item_at = {x: i for i, x in enumerate(ITEMS)}


        def items_to(c, kind, n):
            return c * NI + (item_at[kind, n] + 1 if n >= 0 else 0) + 1

        def tiles_to(c, t):
            return c * NT + t + 2

        def quads_to(c, q):
            return c * NQ + max(q + 1, 0) + 1

        def wait_low(engine, c, q):
            if 0 <= q < DVE_LOW:
                engine.wait_ge(lo_ready_dve, c * DVE_LOW + q + 1)
            else:
                engine.wait_ge(lo_ready, c * (NQ - DVE_LOW) + max(q - DVE_LOW + 1, 0) + 1)

        def mlp_to(c, step):
            return c * MLP + STEPS.index(step) + 2

        def low_part(engine, done, c, q):
            engine.wait_ge(hi_ready, quads_to(c, q))
            engine.wait_ge(item_ready, items_to(c, "tile", QUAD * (q - SPLIT) + QUAD - 1))
            engine.tensor_tensor(
                w_lo[:, q % SPLIT, :], raw[:, q % RAW, :], w_hi[:, q % SPLIT, :], ALU.subtract
            ).then_inc(done, 1)

        @block.sync
        def _(sp):
            sp.dma_start(b1[:], b1t).then_inc(consts_loaded, 16)
            sp.dma_start(b2[:], b2t).then_inc(consts_loaded, 16)
            sp.dma_start(W3[:], W3t).then_inc(consts_loaded, 16)
            sp.dma_start(W1[:], W1g).then_inc(consts_loaded, 16)
            with sp.Fori(0, CHUNKS) as c:
                for q in range(NQ):
                    wait_low(sp, c, q - RAW)
                    for h in range(2):
                        sp.dma_start(raw[E * h : E * h + E, q % RAW, :], param_q[q]).then_inc(raw_loaded[q % RAW], 16)
                sp.wait_ge(quad_summed, quads_to(c, NQ - 1))
                sp.dma_start(W2, W2t).then_inc(W2_loaded, 16)
                sp.wait_ge(z_saved, (c + 1) * NG + 1)
                sp.dma_start(
                    z[DENSE_ROW : DENSE_ROW + DENSE, NG - 1, :], dense_t[:, bass.ds(c * CHUNK, CHUNK)]
                ).then_inc(dense_loaded, 16)

        @block.gpsimd
        def _(pool):
            pool.memset(ident[:], 0.0).then_inc(ident_zero, 1)
            pool.wait_ge(ident_zero, 1)
            pool.affine_select(
                out=ident[:], in_=ident[:], compare_op=ALU.not_equal, fill=1.0, base=0, pattern=[[-1, P]],
                channel_multiplier=1,
            ).then_inc(consts_made, 1)

            def load_indices(c):
                pool.wait_ge(item_ready, items_to(c, "duo", -1))
                pool.sem_inc(pool_waited, 1)
                pool.dma_start(idx[:], ids_t[bass.ds(c, 1)].rearrange("a p f t -> (a p) f t")).then_inc(idx_loaded, 16)
                pool.wait_ge(idx_loaded, (c + 1) * 16)
                pool.sem_inc(pool_waited, 1)

            def gather(c, n):
                k, f, t = n // (2 * BT), n // BT, n % BT
                if n % (2 * BT) == 0:
                    pool.wait_ge(item_ready, items_to(c, "duo", k - STAGE))
                    pool.sem_inc(pool_waited, 1)
                pool.indirect_dma_start(
                    stage[:, k % STAGE, t, E * (f % 2) : E * (f % 2) + E], None, tables[f],
                    bass.IndirectOffsetOnAxis(ap=idx[:, f, t : t + 1], axis=0),
                ).then_inc(gathered[k % STAGE], 16)

            pool.sem_inc(lo_ready, 1)
            with pool.Fori(0, CHUNKS) as c:
                load_indices(c)
                done = 0
                for q in range(DVE_LOW, NQ):
                    needed = 2 * BT * duos_at(QUAD * q - 1)
                    if q == DVE_LOW:
                        needed = 2 * BT * (duos_at(QUAD * (q - 2) - 1) + STAGE)
                    allowed = 2 * BT * (duos_at(QUAD * (q - 1) - 1) + STAGE)
                    upto = max(needed, min(allowed, done + GATHERS, 2 * BT * DUOS))
                    for n in range(done, needed):
                        gather(c, n)
                    low_part(pool, lo_ready, c, q)
                    for n in range(max(done, needed), upto):
                        gather(c, n)
                    done = max(done, upto)
                assert done == 2 * BT * DUOS

        @block.scalar
        def _(act):
            def high_part(c, q):
                act.wait_ge(raw_loaded[q % RAW], 32 * (c * (NQ // RAW) + q // RAW + 1))
                act.wait_ge(item_ready, items_to(c, "tile", QUAD * (q - SPLIT) + QUAD - 1))
                act.activation(w_hi[:, q % SPLIT, :], raw[:, q % RAW, :], ACT.Copy).then_inc(hi_ready, 1)

            def save_duo(c, k):
                i = item_at["duo", k]
                act.wait_ge(item_ready, items_to(c, "duo", k))
                act.activation(emb_t[:, k, :], ring[:, i % Y, :], ACT.Copy).then_inc(duo_saved, 1)
                act.wait_ge(duo_saved, c * DUOS + k + 1)
                act.activation(cols[0:E, k % 2, 0, :], emb_t[0:E, k, :], ACT.Copy).then_inc(cols_hi, 1)
                act.activation(cols[E:P, k % 2, 1, :], emb_t[E:P, k, :], ACT.Copy).then_inc(cols_hi, 1)

            def save_z(c, g):
                act.wait_ge(quad_summed, quads_to(c, min(SLOTS * (g + 1), NQ) - 1))
                act.activation(z[:, g, :], z_ps[:, :], ACT.Copy).then_inc(z_saved, 1)

            act.sem_inc(hi_ready, 1)
            act.sem_inc(z_saved, 1)
            act.sem_inc(mlp_used, 1)
            act.sem_inc(stored, 1)
            with act.Fori(0, CHUNKS) as c:
                high_part(c, 0)
                save_duo(c, 0)
                save_duo(c, 1)
                for q in range(NQ):
                    if q + 1 < NQ:
                        high_part(c, q + 1)
                    if q >= 2 and (q - 2) % SLOTS == SLOTS - 1:
                        save_z(c, (q - 2) // SLOTS)
                    for t in range(QUAD * q, QUAD * q + QUAD):
                        if t in AFTER:
                            save_duo(c, AFTER[t])
                save_z(c, NG - 1)
                act.wait_ge(consts_loaded, 16 * 4)
                for n, (layer, s, m) in enumerate(STEPS):
                    act.wait_ge(mlp_ready, c * MLP + n + 1)
                    if layer == "h1":
                        act.activation(
                            h1[:, s, m, :], ring[:, m // 2, SUB * (m % 2) : SUB * (m % 2) + SUB], ACT.Relu,
                            bias=b1[:, m : m + 1],
                        ).then_inc(mlp_used, 1)
                    elif layer == "h2":
                        act.activation(
                            h2[:, s, m, :], ring[:, 2, SUB * m : SUB * m + SUB], ACT.Relu, bias=b2[:, m : m + 1]
                        ).then_inc(mlp_used, 1)
                    else:
                        if s == 0:
                            act.wait_ge(stored, 16 * SUBS * c + 1)
                        act.activation(y_out[:, s, :], z_ps[0:1, SUB * s : SUB * s + SUB], ACT.Copy).then_inc(
                            mlp_used, 1
                        )
                        act.wait_ge(mlp_used, mlp_to(c, ("y", s, 0)))
                        act.dma_start(out_v[bass.ds(c * SUBS + s, 1), :], y_out[:, s, :]).then_inc(stored, 16)
            act.wait_ge(stored, 16 * CHUNKS * SUBS + 1)

        @block.vector
        def _(dve):
            dve.memset(sel[:], 0.0).then_inc(sel_zero, 1)
            dve.wait_ge(sel_zero, 1)
            dve.memset(sel[0:E, 30:31], 1.0).then_inc(consts_made, 1)
            dve.memset(sel[E:P, 31:32], 1.0).then_inc(consts_made, 1)
            def low_cols(c, k, h):
                dve.wait_ge(cols_hi, 2 * (c * DUOS + k) + h + 1)
                here, there = slice(E * h, E * h + E), slice(E - E * h, P - E * h)
                dve.tensor_tensor(
                    cols[there, k % 2, h, :], emb_t[here, k, :], cols[here, k % 2, h, :], ALU.subtract
                ).then_inc(cols_ready, 1)

            dve.sem_inc(tile_done, 1)
            with dve.Fori(0, CHUNKS) as c:
                low_part(dve, lo_ready_dve, c, 0)
                low_cols(c, 0, 0)
                low_cols(c, 0, 1)
                low_cols(c, 1, 0)
                low_cols(c, 1, 1)
                for t in range(NT):
                    dve.wait_ge(item_ready, items_to(c, "tile", t))
                    dve.wait_ge(quad_summed, quads_to(c, (t - PROD) // QUAD))
                    dve.tensor_tensor(
                        prod[:, t % PROD, :], ring[:, item_at["tile", t] % Y, :], emb_t[:, TILES[t][1], :], ALU.mult
                    ).then_inc(tile_done, 1)
                    if t % QUAD == LOW_AT and t // QUAD + 1 < DVE_LOW:
                        low_part(dve, lo_ready_dve, c, t // QUAD + 1)
                    for k, h in LOW_AFTER.get(t, ()):
                        low_cols(c, k, h)

        @block.tensor
        def _(pe):
            pe.wait_ge(consts_made, 3)

            def slot_free(c, i):
                if i >= Y:
                    kind, n = ITEMS[i - Y]
                    if kind == "duo":
                        pe.wait_ge(duo_saved, c * DUOS + n + 1)
                    else:
                        pe.wait_ge(tile_done, tiles_to(c, n))

            def transpose_duo(c, k):
                i = item_at["duo", k]
                pe.wait_ge(gathered[k % STAGE], 16 * 2 * BT * (c * (DUOS // STAGE) + k // STAGE + 1))
                slot_free(c, i)
                for t in range(BT):
                    mm = pe.transpose(ring[:, i % Y, P * t : P * t + P], stage[:, k % STAGE, t, :], ident[:])
                mm.then_inc(item_ready, 1)

            def multiply(c, t):
                i = item_at["tile", t]
                col, _ = TILES[t]
                q, j = divmod(t, QUAD)
                if t in FIRST:
                    pe.wait_ge(cols_ready, 2 * (c * DUOS + FIRST[t] + 1))
                if j == 0:
                    wait_low(pe, c, q)
                slot_free(c, i)
                for w in (w_lo, w_hi):
                    for s in range(SUBS):
                        mm = pe.matmul(
                            ring[:, i % Y, SUB * s : SUB * s + SUB], w[:, q % SPLIT, P * j : P * j + P],
                            cols[:, col // 2 % 2, col % 2, SUB * s : SUB * s + SUB],
                            start=(w is w_lo), stop=(w is w_hi),
                        )
                mm.then_inc(item_ready, 1)

            def sum_products(c, q):
                pe.wait_ge(tile_done, tiles_to(c, QUAD * q + QUAD - 1))
                g, slot = divmod(q, SLOTS)
                if slot == 0:
                    pe.wait_ge(z_saved, c * NG + g + 1)
                    if g == 0:
                        pe.wait_ge(mlp_used, c * MLP + 1)
                last = slot == SLOTS - 1 or q == NQ - 1
                for s in range(SUBS):
                    for j in range(QUAD):
                        mm = pe.matmul(
                            z_ps[32 * j : 32 * j + 32, SUB * s : SUB * s + SUB], sel[:, 30 - 2 * slot : 62 - 2 * slot],
                            prod[:, (QUAD * q + j) % PROD, SUB * s : SUB * s + SUB], start=(slot == 0), stop=last,
                        )
                mm.then_inc(quad_summed, 1)

            def mlp(c):
                pe.wait_ge(consts_loaded, 16 * 4)
                pe.wait_ge(z_saved, (c + 1) * NG + 1)
                pe.wait_ge(dense_loaded, (c + 1) * 16)
                pe.wait_ge(W2_loaded, (c + 1) * 16)
                for n, (layer, s, m) in enumerate(STEPS):
                    if layer == "h1":
                        if s:
                            pe.wait_ge(mlp_used, mlp_to(c, ("h1", s - 1, m)))
                        for g in range(NG):
                            mm = pe.matmul(
                                ring[:, m // 2, SUB * (m % 2) : SUB * (m % 2) + SUB], W1[:, g, P * m : P * m + P],
                                z[:, g, SUB * s : SUB * s + SUB], start=(g == 0), stop=(g == NG - 1),
                            )
                    elif layer == "h2":
                        before = ("h2", s - 1, m) if s else ("h1", s, H1 // P - 1)
                        pe.wait_ge(mlp_used, mlp_to(c, before))
                        for g in range(H1 // P):
                            mm = pe.matmul(
                                ring[:, 2, SUB * m : SUB * m + SUB], W2[:, g, P * m : P * m + P], h1[:, s, g, :],
                                start=(g == 0), stop=(g == H1 // P - 1),
                            )
                    else:
                        pe.wait_ge(mlp_used, mlp_to(c, ("h2", s, H2 // P - 1)))
                        for g in range(H2 // P):
                            mm = pe.matmul(
                                z_ps[0:1, SUB * s : SUB * s + SUB], W3[:, g : g + 1], h2[:, s, g, :],
                                start=(g == 0), stop=(g == H2 // P - 1),
                            )
                    mm.then_inc(mlp_ready, 1)

            pe.sem_inc(item_ready, 1)
            pe.sem_inc(quad_summed, 1)
            with pe.Fori(0, CHUNKS) as c:
                transpose_duo(c, 0)
                transpose_duo(c, 1)
                for q in range(NQ):
                    for t in range(QUAD * q, QUAD * q + QUAD):
                        multiply(c, t)
                        if t in AFTER:
                            transpose_duo(c, AFTER[t])
                    if q:
                        sum_products(c, q - 1)
                sum_products(c, NQ - 1)
                mlp(c)


def kernel(**inputs):
    import concourse.bacc as bacc
    from concourse.bass_utils import run_bass_kernel_spmd

    nc = bacc.Bacc("TRN2", target_bir_lowering=False, num_devices=1)
    W = {k: np.asarray(v) for k, v in inputs.items()}

    param = W["L0_rec_param"]
    param_q = np.zeros((NQ, E, QUAD, 2, E), param.dtype)
    W1g = np.zeros((P, NG, H1), W["W_top1"].dtype)
    for t, (c, k) in enumerate(TILES):
        q, j = divmod(t, QUAD)
        g, slot = divmod(q, SLOTS)
        for h in range(2):
            r = 2 * k + h
            if r < c:
                param_q[q, :, j, h] = param[:, pair_index(r, c)]
                W1g[32 * j + 2 * slot + h, g] = W["W_top1"][pair_index(r, c)]
    W1g[DENSE_ROW : DENSE_ROW + DENSE, NG - 1] = W["W_top1"][-DENSE:]

    arrays = {
        "dense_t": np.ascontiguousarray(W["dense_ctx"].T),
        "ids_t": np.ascontiguousarray(W["ids"].reshape(CHUNKS, BT, P, FIELDS).transpose(0, 2, 3, 1)),
        "param_q": param_q.reshape(NQ, E, QUAD * P),
        "W1g": W1g,
        "b1t": np.ascontiguousarray(W["b_top1"].reshape(H1 // P, P).T),
        "W2t": np.ascontiguousarray(W["W_top2"].reshape(H1 // P, P, H2).transpose(1, 0, 2)),
        "b2t": np.ascontiguousarray(W["b_top2"].reshape(H2 // P, P).T),
        "W3t": np.ascontiguousarray(W["W_top3"].reshape(H2 // P, P).T),
    }
    for f in range(FIELDS):
        arrays[f"tbl_{f}"] = np.ascontiguousarray(W[f"tbl_{f}"])
    ap = {
        name: nc.dram_tensor(name, a.shape, mybir.dt.from_np(a.dtype), kind="ExternalInput").ap()
        for name, a in arrays.items()
    }
    out = nc.dram_tensor("out", (B, 1), F32, kind="ExternalOutput").ap()
    tables = [ap[f"tbl_{f}"] for f in range(FIELDS)]
    fm_mlp_kernel(
        nc, ap["dense_t"], ap["ids_t"], tables, ap["param_q"], ap["W1g"], ap["b1t"], ap["W2t"], ap["b2t"], ap["W3t"],
        out,
    )
    r = run_bass_kernel_spmd(nc, [arrays], core_ids=[0])
    return r.results[0]["out"]
```

```python
from contextlib import ExitStack

import concourse.bass as bass
import numpy as np
from concourse import mybir

F32 = mybir.dt.float32
F32R = mybir.dt.float32r
I32 = mybir.dt.int32
ALU = mybir.AluOpType
ACT = mybir.ActivationFunctionType

P = 128
FIELDS = 40
E = 64
B = 2048
CHUNK = 1024
CHUNKS = B // CHUNK
SUB = 512
SUBS = CHUNK // SUB
BT = CHUNK // P
DENSE = 16
H1, H2 = 512, 256

DUOS = FIELDS // 2
TILES = [(c, k) for c in range(1, FIELDS) for k in range((c + 1) // 2)]
NT = len(TILES)
FIRST = {k * k: k for k in range(DUOS)}
QUAD = 4
NQ = NT // QUAD
SLOTS = P // QUAD // 2
NG = -(-NQ // SLOTS)
DENSE_ROW = 2 * (NQ - (NG - 1) * SLOTS)
assert NT == DUOS * DUOS and NQ * QUAD == NT and DENSE_ROW + DENSE <= 32

Y = 3
PROD = 2 * QUAD
STAGE = 4
PREFETCH = 4
DVE_LOW = 36
LOW_AT = 1
GATHERS = 4
RAW = 2
SPLIT = 2

LEAD, SHORT, LATE = 12, 8, 10
AFTER = {max(k * k - 1, (k + 1) * (k + 1) - (LEAD if k > LATE else SHORT)): k + 1 for k in range(1, DUOS - 1)}
ITEMS = [("duo", 0), ("duo", 1)]
for _t in range(NT):
    ITEMS.append(("tile", _t))
    if _t in AFTER:
        ITEMS.append(("duo", AFTER[_t]))
NI = len(ITEMS)
LOW_AFTER = {}
for _a, _k in AFTER.items():
    if _k == 1:
        continue
    _last = _k * _k - 1
    _ends = [t for t in range(_a + 2, _last + 1) if t % QUAD == QUAD - 1]
    if _k <= LATE + 1:
        _places = min(_a + 2, _last), min(_a + 4, _last)
    else:
        _places = (_ends[0], _ends[1]) if len(_ends) > 1 else (_last, _last)
    for _h, _t in enumerate(_places):
        LOW_AFTER.setdefault(_t, []).append((_k, _h))


def duos_at(t):
    return 2 + sum(a <= t for a in AFTER) if t >= 0 else 0


STEPS = [("h1", s, m) for s in range(SUBS) for m in range(H1 // P)]
STEPS += [("h2", s, m) for s in range(SUBS) for m in range(H2 // P)]
STEPS += [("y", s, 0) for s in range(SUBS)]
MLP = len(STEPS)


def pair_index(r, c):
    return r * (2 * FIELDS - 1 - r) // 2 + c - r - 1


def fm_mlp_kernel(nc, dense_t, ids_t, tables, param_q, W1g, b1t, W2t, b2t, W3t, out):
    out_v = out.rearrange("(a n) o -> a (n o)", n=SUB)
    with ExitStack() as ctx:

        def sb(name, shape, dt=F32):
            return ctx.enter_context(nc.sbuf_tensor(name, shape, dt))

        def sem(name):
            return ctx.enter_context(nc.semaphore(name))

        ident = sb("ident", [P, P])
        sel = sb("sel", [P, 62])
        idx = sb("idx", [P, FIELDS, BT], I32)
        stage = sb("stage", [P, STAGE, BT, 2 * E])
        emb_t = sb("emb_t", [P, DUOS, CHUNK])
        cols = sb("cols", [P, 2, 2, CHUNK], F32R)
        raw = sb("raw", [P, RAW, QUAD * P])
        w_hi = sb("w_hi", [P, SPLIT, QUAD * P], F32R)
        w_lo = sb("w_lo", [P, SPLIT, QUAD * P], F32R)
        prod = sb("prod", [P, PROD, CHUNK])
        z = sb("z", [P, NG, CHUNK])
        W1 = sb("W1", [P, NG, H1])
        W3 = sb("W3", [P, H2 // P])
        b1 = sb("b1", [P, H1 // P])
        b2 = sb("b2", [P, H2 // P])
        y_out = sb("y_out", [1, SUBS, SUB])
        h1 = prod[:, 0:4, :].rearrange("p (s a) (b n) -> p s (a b) n", s=SUBS, n=SUB)
        h2 = prod[:, 4:6, :].rearrange("p s (b n) -> p s b n", n=SUB)
        W2 = prod[:, 6, :].rearrange("p (g n) -> p g n", n=H2)

        ring = ctx.enter_context(nc.psum_tensor("ring", [P, Y, CHUNK], F32))
        z_ps = ctx.enter_context(nc.psum_tensor("z_ps", [P, CHUNK], F32))

        consts_loaded = sem("consts_loaded")
        consts_made = sem("consts_made")
        ident_zero = sem("ident_zero")
        sel_zero = sem("sel_zero")
        idx_loaded = sem("idx_loaded")
        gathered = [sem(f"gathered{i}") for i in range(STAGE)]
        pool_waited = sem("pool_waited")
        cols_hi = sem("cols_hi")
        raw_loaded = [sem(f"raw_loaded{i}") for i in range(RAW)]
        hi_ready = sem("hi_ready")
        lo_ready = sem("lo_ready")
        lo_ready_dve = sem("lo_ready_dve")
        item_ready = sem("item_ready")
        tile_done = sem("tile_done")
        duo_saved = sem("duo_saved")
        cols_ready = sem("cols_ready")
        quad_summed = sem("quad_summed")
        z_saved = sem("z_saved")
        dense_loaded = sem("dense_loaded")
        W2_loaded = sem("W2_loaded")
        mlp_ready = sem("mlp_ready")
        mlp_used = sem("mlp_used")
        stored = sem("stored")

        block = ctx.enter_context(nc.Block())

        item_at = {x: i for i, x in enumerate(ITEMS)}


        def items_to(c, kind, n):
            return c * NI + (item_at[kind, n] + 1 if n >= 0 else 0) + 1

        def duo_before(c, k):
            return items_to(c, "duo", DUOS + k - STAGE) - NI if not isinstance(c, int) else 1

        def tiles_to(c, t):
            return c * NT + t + 2

        def quads_to(c, q):
            return c * NQ + max(q + 1, 0) + 1

        def cols_to(c, k, h):
            return c * (FIELDS - 1) + 2 * k + h

        def wait_low(engine, c, q):
            if 0 <= q < DVE_LOW:
                engine.wait_ge(lo_ready_dve, c * DVE_LOW + q + 1)
            else:
                engine.wait_ge(lo_ready, c * (NQ - DVE_LOW) + max(q - DVE_LOW + 1, 0) + 1)

        def mlp_to(c, step):
            return c * MLP + STEPS.index(step) + 2

        def low_part(engine, done, c, q):
            engine.wait_ge(hi_ready, quads_to(c, q))
            engine.wait_ge(item_ready, items_to(c, "tile", QUAD * (q - SPLIT) + QUAD - 1))
            engine.tensor_tensor(
                w_lo[:, q % SPLIT, :], raw[:, q % RAW, :], w_hi[:, q % SPLIT, :], ALU.subtract
            ).then_inc(done, 1)

        @block.sync
        def _(sp):
            sp.dma_start(b1[:], b1t).then_inc(consts_loaded, 16)
            sp.dma_start(b2[:], b2t).then_inc(consts_loaded, 16)
            sp.dma_start(W3[:], W3t).then_inc(consts_loaded, 16)
            sp.wait_ge(idx_loaded, 16)
            sp.dma_start(W1[:], W1g).then_inc(consts_loaded, 16)

            def load_weights(q):
                for h in range(2):
                    sp.dma_start(raw[E * h : E * h + E, q % RAW, :], param_q[q]).then_inc(raw_loaded[q % RAW], 16)

            load_weights(0)
            with sp.Fori(0, CHUNKS) as c:
                for q in range(1, NQ):
                    wait_low(sp, c, q - RAW)
                    load_weights(q)
                wait_low(sp, c, NQ - RAW)
                load_weights(0)
                sp.wait_ge(quad_summed, quads_to(c, NQ - 1))
                sp.dma_start(W2, W2t).then_inc(W2_loaded, 16)
                sp.wait_ge(z_saved, (c + 1) * NG + 1)
                sp.dma_start(
                    z[DENSE_ROW : DENSE_ROW + DENSE, NG - 1, :], dense_t[:, bass.ds(c * CHUNK, CHUNK)]
                ).then_inc(dense_loaded, 16)

        @block.gpsimd
        def _(pool):
            pool.memset(ident[:], 0.0).then_inc(ident_zero, 1)
            pool.wait_ge(ident_zero, 1)
            pool.affine_select(
                out=ident[:], in_=ident[:], compare_op=ALU.not_equal, fill=1.0, base=0, pattern=[[-1, P]],
                channel_multiplier=1,
            ).then_inc(consts_made, 1)

            def load_indices(c):
                pool.dma_start(idx[:], ids_t[bass.ds(c, 1)].rearrange("a p f t -> (a p) f t")).then_inc(idx_loaded, 16)
                pool.wait_ge(idx_loaded, (c + 1) * 16)
                pool.sem_inc(pool_waited, 1)

            def gather(c, n):
                k, f, t = n // (2 * BT), n // BT, n % BT
                if n % (2 * BT) == 0:
                    pool.wait_ge(item_ready, items_to(c, "duo", k - STAGE) if k >= 2 else duo_before(c, k))
                    pool.sem_inc(pool_waited, 1)
                pool.indirect_dma_start(
                    stage[:, k % STAGE, t, E * (f % 2) : E * (f % 2) + E], None, tables[f],
                    bass.IndirectOffsetOnAxis(ap=idx[:, f, t : t + 1], axis=0),
                ).then_inc(gathered[k % STAGE], 16)

            pool.sem_inc(lo_ready, 1)
            load_indices(0)
            for n in range(2 * 2 * BT):
                gather(0, n)
            with pool.Fori(0, CHUNKS) as c:
                done = 2 * 2 * BT
                for q in range(DVE_LOW, NQ):
                    needed = 2 * BT * duos_at(QUAD * q - 1)
                    if q == DVE_LOW:
                        needed = 2 * BT * (duos_at(QUAD * (q - 2) - 1) + STAGE)
                    allowed = 2 * BT * (duos_at(QUAD * (q - 1) - 1) + STAGE)
                    upto = max(needed, min(allowed, done + GATHERS, 2 * BT * DUOS))
                    for n in range(done, needed):
                        gather(c, n)
                    low_part(pool, lo_ready, c, q)
                    for n in range(max(done, needed), upto):
                        gather(c, n)
                    done = max(done, upto)
                assert done == 2 * BT * DUOS
                pool.wait_ge(item_ready, items_to(c, "duo", DUOS - 1))
                pool.sem_inc(pool_waited, 1)
                load_indices(c + 1)
                for n in range(2 * 2 * BT):
                    gather(c + 1, n)

        @block.scalar
        def _(act):
            def high_part(c, q):
                act.wait_ge(raw_loaded[q % RAW], 32 * (c * (NQ // RAW) + q // RAW + 1))
                act.wait_ge(item_ready, items_to(c, "tile", QUAD * (q - SPLIT) + QUAD - 1))
                act.activation(w_hi[:, q % SPLIT, :], raw[:, q % RAW, :], ACT.Copy).then_inc(hi_ready, 1)

            def save_duo(c, k):
                i = item_at["duo", k]
                act.wait_ge(item_ready, items_to(c, "duo", k))
                act.activation(emb_t[:, k, :], ring[:, i % Y, :], ACT.Copy).then_inc(duo_saved, 1)
                act.wait_ge(duo_saved, c * DUOS + k + 1)
                if k:
                    act.activation(cols[0:E, k % 2, 0, :], emb_t[0:E, k, :], ACT.Copy).then_inc(cols_hi, 1)
                act.activation(cols[E:P, k % 2, 1, :], emb_t[E:P, k, :], ACT.Copy).then_inc(cols_hi, 1)

            def save_z(c, g):
                act.wait_ge(quad_summed, quads_to(c, min(SLOTS * (g + 1), NQ) - 1))
                act.activation(z[:, g, :], z_ps[:, :], ACT.Copy).then_inc(z_saved, 1)

            act.sem_inc(hi_ready, 1)
            act.sem_inc(z_saved, 1)
            act.sem_inc(mlp_used, 1)
            act.sem_inc(stored, 1)
            high_part(0, 0)
            save_duo(0, 0)
            save_duo(0, 1)
            with act.Fori(0, CHUNKS) as c:
                for q in range(NQ):
                    if q + 1 < NQ:
                        high_part(c, q + 1)
                    if q >= 2 and (q - 2) % SLOTS == SLOTS - 1:
                        save_z(c, (q - 2) // SLOTS)
                    for t in range(QUAD * q, QUAD * q + QUAD):
                        if t in AFTER:
                            save_duo(c, AFTER[t])
                save_z(c, NG - 1)
                act.wait_ge(consts_loaded, 16 * 4)
                for n, (layer, s, m) in enumerate(STEPS):
                    if n == SUBS * (H1 // P):
                        save_duo(c + 1, 0)
                        save_duo(c + 1, 1)
                        high_part(c + 1, 0)
                    act.wait_ge(mlp_ready, c * MLP + n + 1)
                    if layer == "h1":
                        act.activation(
                            h1[:, s, m, :], ring[:, m // 2, SUB * (m % 2) : SUB * (m % 2) + SUB], ACT.Relu,
                            bias=b1[:, m : m + 1],
                        ).then_inc(mlp_used, 1)
                    elif layer == "h2":
                        act.activation(
                            h2[:, s, m, :], ring[:, 2, SUB * m : SUB * m + SUB], ACT.Relu, bias=b2[:, m : m + 1]
                        ).then_inc(mlp_used, 1)
                    else:
                        if s == 0:
                            act.wait_ge(stored, 16 * SUBS * c + 1)
                        act.activation(y_out[:, s, :], z_ps[0:1, SUB * s : SUB * s + SUB], ACT.Copy).then_inc(
                            mlp_used, 1
                        )
                        act.wait_ge(mlp_used, mlp_to(c, ("y", s, 0)))
                        act.dma_start(out_v[bass.ds(c * SUBS + s, 1), :], y_out[:, s, :]).then_inc(stored, 16)
            act.wait_ge(stored, 16 * CHUNKS * SUBS + 1)

        @block.vector
        def _(dve):
            dve.memset(sel[:], 0.0).then_inc(sel_zero, 1)
            dve.wait_ge(sel_zero, 1)
            dve.memset(sel[0:E, 30:31], 1.0).then_inc(consts_made, 1)
            dve.memset(sel[E:P, 31:32], 1.0).then_inc(consts_made, 1)
            def low_cols(c, k, h):
                dve.wait_ge(cols_hi, cols_to(c, k, h))
                here, there = slice(E * h, E * h + E), slice(E - E * h, P - E * h)
                dve.tensor_tensor(
                    cols[there, k % 2, h, :], emb_t[here, k, :], cols[here, k % 2, h, :], ALU.subtract
                ).then_inc(cols_ready, 1)

            dve.sem_inc(tile_done, 1)
            for k, h in ((0, 1), (1, 0), (1, 1)):
                low_cols(0, k, h)
            low_part(dve, lo_ready_dve, 0, 0)
            with dve.Fori(0, CHUNKS) as c:
                for t in range(NT):
                    dve.wait_ge(item_ready, items_to(c, "tile", t))
                    dve.wait_ge(quad_summed, quads_to(c, (t - PROD) // QUAD))
                    dve.tensor_tensor(
                        prod[:, t % PROD, :], ring[:, item_at["tile", t] % Y, :], emb_t[:, TILES[t][1], :], ALU.mult
                    ).then_inc(tile_done, 1)
                    if t % QUAD == LOW_AT and t // QUAD + 1 < DVE_LOW:
                        low_part(dve, lo_ready_dve, c, t // QUAD + 1)
                    for k, h in LOW_AFTER.get(t, ()):
                        low_cols(c, k, h)
                for k, h in ((0, 1), (1, 0), (1, 1)):
                    low_cols(c + 1, k, h)
                low_part(dve, lo_ready_dve, c + 1, 0)

        @block.tensor
        def _(pe):
            pe.wait_ge(consts_made, 3)

            def slot_free(c, i):
                if i >= Y:
                    kind, n = ITEMS[i - Y]
                    if kind == "duo":
                        pe.wait_ge(duo_saved, c * DUOS + n + 1)
                    else:
                        pe.wait_ge(tile_done, tiles_to(c, n))

            def transpose_duo(c, k):
                i = item_at["duo", k]
                pe.wait_ge(gathered[k % STAGE], 16 * 2 * BT * (c * (DUOS // STAGE) + k // STAGE + 1))
                slot_free(c, i)
                for t in range(BT):
                    mm = pe.transpose(ring[:, i % Y, P * t : P * t + P], stage[:, k % STAGE, t, :], ident[:])
                mm.then_inc(item_ready, 1)

            def multiply(c, t):
                i = item_at["tile", t]
                col, _ = TILES[t]
                q, j = divmod(t, QUAD)
                if t in FIRST:
                    pe.wait_ge(cols_ready, cols_to(c, FIRST[t], 1))
                if j == 0:
                    wait_low(pe, c, q)
                slot_free(c, i)
                for w in (w_lo, w_hi):
                    for s in range(SUBS):
                        mm = pe.matmul(
                            ring[:, i % Y, SUB * s : SUB * s + SUB], w[:, q % SPLIT, P * j : P * j + P],
                            cols[:, col // 2 % 2, col % 2, SUB * s : SUB * s + SUB],
                            start=(w is w_lo), stop=(w is w_hi),
                        )
                mm.then_inc(item_ready, 1)

            def sum_products(c, q):
                pe.wait_ge(tile_done, tiles_to(c, QUAD * q + QUAD - 1))
                g, slot = divmod(q, SLOTS)
                if slot == 0:
                    pe.wait_ge(z_saved, c * NG + g + 1)
                    if g == 0:
                        pe.wait_ge(mlp_used, c * MLP + 1)
                last = slot == SLOTS - 1 or q == NQ - 1
                for s in range(SUBS):
                    for j in range(QUAD):
                        mm = pe.matmul(
                            z_ps[32 * j : 32 * j + 32, SUB * s : SUB * s + SUB], sel[:, 30 - 2 * slot : 62 - 2 * slot],
                            prod[:, (QUAD * q + j) % PROD, SUB * s : SUB * s + SUB], start=(slot == 0), stop=last,
                        )
                mm.then_inc(quad_summed, 1)

            def h1_part(c, n, groups):
                _, s, m = STEPS[n]
                for g in groups:
                    mm = pe.matmul(
                        ring[:, m // 2, SUB * (m % 2) : SUB * (m % 2) + SUB], W1[:, g, P * m : P * m + P],
                        z[:, g, SUB * s : SUB * s + SUB], start=(g == 0), stop=(g == NG - 1),
                    )
                if NG - 1 in groups:
                    mm.then_inc(mlp_ready, 1)

            def mlp_start(c):
                assert NI % Y == 0 and STEPS[:2] == [("h1", 0, 0), ("h1", 0, 1)]
                pe.wait_ge(consts_loaded, 16 * 4)
                pe.wait_ge(z_saved, c * NG + NG)
                slot_free(c, NI)
                h1_part(c, 0, range(NG - 1))
                sum_products(c, NQ - 1)
                h1_part(c, 1, range(NG - 1))
                pe.wait_ge(z_saved, (c + 1) * NG + 1)
                pe.wait_ge(dense_loaded, (c + 1) * 16)
                h1_part(c, 0, [NG - 1])
                h1_part(c, 1, [NG - 1])

            def mlp_rest(c):
                for n, (layer, s, m) in enumerate(STEPS):
                    if n < 2:
                        continue
                    if layer == "h1":
                        if s:
                            pe.wait_ge(mlp_used, mlp_to(c, ("h1", s - 1, m)))
                        h1_part(c, n, range(NG))
                        continue
                    if layer == "h2":
                        if (s, m) == (0, 0):
                            pe.wait_ge(W2_loaded, (c + 1) * 16)
                            for k in range(2):
                                pe.wait_ge(mlp_used, mlp_to(c, ("h1", SUBS - 1, 2 * k + 1)))
                                transpose_duo(c + 1, k)
                        before = ("h2", s - 1, m) if s else ("h1", s, H1 // P - 1)
                        pe.wait_ge(mlp_used, mlp_to(c, before))
                        for g in range(H1 // P):
                            mm = pe.matmul(
                                ring[:, 2, SUB * m : SUB * m + SUB], W2[:, g, P * m : P * m + P], h1[:, s, g, :],
                                start=(g == 0), stop=(g == H1 // P - 1),
                            )
                    else:
                        pe.wait_ge(mlp_used, mlp_to(c, ("h2", s, H2 // P - 1)))
                        for g in range(H2 // P):
                            mm = pe.matmul(
                                z_ps[0:1, SUB * s : SUB * s + SUB], W3[:, g : g + 1], h2[:, s, g, :],
                                start=(g == 0), stop=(g == H2 // P - 1),
                            )
                    mm.then_inc(mlp_ready, 1)

            pe.sem_inc(item_ready, 1)
            pe.sem_inc(quad_summed, 1)
            transpose_duo(0, 0)
            transpose_duo(0, 1)
            with pe.Fori(0, CHUNKS) as c:
                for q in range(NQ):
                    for t in range(QUAD * q, QUAD * q + QUAD):
                        multiply(c, t)
                        if t in AFTER:
                            transpose_duo(c, AFTER[t])
                    if q:
                        sum_products(c, q - 1)
                mlp_start(c)
                mlp_rest(c)


def kernel(**inputs):
    import concourse.bacc as bacc
    from concourse.bass_utils import run_bass_kernel_spmd

    nc = bacc.Bacc("TRN2", target_bir_lowering=False, num_devices=1)
    W = {k: np.asarray(v) for k, v in inputs.items()}

    param = W["L0_rec_param"]
    param_q = np.zeros((NQ, E, QUAD, 2, E), param.dtype)
    W1g = np.zeros((P, NG, H1), W["W_top1"].dtype)
    for t, (c, k) in enumerate(TILES):
        q, j = divmod(t, QUAD)
        g, slot = divmod(q, SLOTS)
        for h in range(2):
            r = 2 * k + h
            if r < c:
                param_q[q, :, j, h] = param[:, pair_index(r, c)]
                W1g[32 * j + 2 * slot + h, g] = W["W_top1"][pair_index(r, c)]
    W1g[DENSE_ROW : DENSE_ROW + DENSE, NG - 1] = W["W_top1"][-DENSE:]

    ids_t = W["ids"].reshape(CHUNKS, BT, P, FIELDS).transpose(0, 2, 3, 1)
    arrays = {
        "dense_t": np.ascontiguousarray(W["dense_ctx"].T),
        "ids_t": np.concatenate([ids_t, ids_t[:1]]),
        "param_q": param_q.reshape(NQ, E, QUAD * P),
        "W1g": W1g,
        "b1t": np.ascontiguousarray(W["b_top1"].reshape(H1 // P, P).T),
        "W2t": np.ascontiguousarray(W["W_top2"].reshape(H1 // P, P, H2).transpose(1, 0, 2)),
        "b2t": np.ascontiguousarray(W["b_top2"].reshape(H2 // P, P).T),
        "W3t": np.ascontiguousarray(W["W_top3"].reshape(H2 // P, P).T),
    }
    for f in range(FIELDS):
        arrays[f"tbl_{f}"] = np.ascontiguousarray(W[f"tbl_{f}"])
    ap = {
        name: nc.dram_tensor(name, a.shape, mybir.dt.from_np(a.dtype), kind="ExternalInput").ap()
        for name, a in arrays.items()
    }
    out = nc.dram_tensor("out", (B, 1), F32, kind="ExternalOutput").ap()
    tables = [ap[f"tbl_{f}"] for f in range(FIELDS)]
    fm_mlp_kernel(
        nc, ap["dense_t"], ap["ids_t"], tables, ap["param_q"], ap["W1g"], ap["b1t"], ap["W2t"], ap["b2t"], ap["W3t"],
        out,
    )
    r = run_bass_kernel_spmd(nc, [arrays], core_ids=[0])
    return r.results[0]["out"]
```

```python
from contextlib import ExitStack

import concourse.bass as bass
import numpy as np
from concourse import mybir


F32 = mybir.dt.float32
F32R = mybir.dt.float32r
I32 = mybir.dt.int32
ALU = mybir.AluOpType
ACT = mybir.ActivationFunctionType

P = 128
FIELDS = 40
E = 64
B = 2048
CHUNK = 1024
CHUNKS = B // CHUNK
SUB = 512
SUBS = CHUNK // SUB
BT = CHUNK // P
DENSE = 16
H1, H2 = 512, 256

DUOS = FIELDS // 2
TILES = [(c, k) for c in range(1, FIELDS) for k in range((c + 1) // 2)]
NT = len(TILES)
FIRST = {k * k + h * k: (k, h) for k in range(1, DUOS) for h in range(2)} | {0: (0, 1)}
assert all(TILES[t] == (2 * k + h, 0) for t, (k, h) in FIRST.items())
QUAD = 4
NQ = NT // QUAD
SLOTS = P // QUAD // 2
NG = -(-NQ // SLOTS)
DENSE_ROW = 2 * (NQ - (NG - 1) * SLOTS)
assert NT == DUOS * DUOS and NQ * QUAD == NT and DENSE_ROW + DENSE <= 32

Y = 3
PROD = 2 * QUAD
STAGE = 4
RAW = 3
SPLIT = 3
AHEAD = 2

EARLY = 2
GATHERS = 4
DVE_LOW = 20
LOW_AT = 1
assert DVE_LOW <= NQ - RAW and DUOS % STAGE == 0

LEAD = 8
AFTER = {max(k * k - 1, (k + 1) * (k + 1) - LEAD): k + 1 for k in range(EARLY - 1, DUOS - 1)}
ITEMS = [("duo", _k) for _k in range(EARLY)]
for _t in range(NT):
    ITEMS.append(("tile", _t))
    if _t in AFTER:
        ITEMS.append(("duo", AFTER[_t]))
NI = len(ITEMS)
assert NI % Y == 0 and EARLY < Y
LOW_AFTER = {}
for _a, _k in AFTER.items():
    for _h in range(2):
        LOW_AFTER.setdefault(min(_a + 2 + 2 * _h, _k * _k + _h * _k - 1), []).append((_k, _h))

DUO_GATHERS = 2 * BT


def duos_at(t):
    return EARLY + sum(a <= t for a in AFTER)


STEPS = [("h1", s, m) for s in range(SUBS) for m in range(H1 // P)]
STEPS += [("h2", s, m) for s in range(SUBS) for m in range(H2 // P)]
STEPS += [("y", s, 0) for s in range(SUBS)]
MLP = len(STEPS)

EARLY_COLS = [(k, h) for k in range(EARLY) for h in range(2)][1:]


def pair_index(r, c):
    return r * (2 * FIELDS - 1 - r) // 2 + c - r - 1


def fm_mlp_kernel(nc, dense_t, ids_t, tables, param_q, W1g, b1t, W2t, b2t, W3t, out):
    out_v = out.rearrange("(a n) o -> a (n o)", n=SUB)
    with ExitStack() as ctx:

        def sb(name, shape, dt=F32):
            return ctx.enter_context(nc.sbuf_tensor(name, shape, dt))

        def sem(name):
            return ctx.enter_context(nc.semaphore(name))

        ident = sb("ident", [P, P])
        sel = sb("sel", [P, 62])
        idx = sb("idx", [P, FIELDS, BT], I32)
        stage = sb("stage", [P, STAGE, BT, 2 * E])
        emb_t = sb("emb_t", [P, DUOS, CHUNK])
        cols = sb("cols", [P, 2, 2, CHUNK], F32R)
        raw = sb("raw", [P, RAW, QUAD * P])
        w_hi = sb("w_hi", [P, SPLIT, QUAD * P], F32R)
        w_lo = sb("w_lo", [P, SPLIT, QUAD * P], F32R)
        prod = sb("prod", [P, PROD, CHUNK])
        z = sb("z", [P, NG, CHUNK])
        W1 = sb("W1", [P, NG, H1])
        W3 = sb("W3", [P, H2 // P])
        b1 = sb("b1", [P, H1 // P])
        b2 = sb("b2", [P, H2 // P])
        h1 = prod[:, 0:4, :].rearrange("p (s a) (b n) -> p s (a b) n", s=SUBS, n=SUB)
        h2 = prod[:, 4:6, :].rearrange("p s (b n) -> p s b n", n=SUB)
        W2 = prod[:, 6, :].rearrange("p (g n) -> p g n", n=H2)
        y_out = prod[0:1, PROD - 1, :].rearrange("p (s n) -> p s n", n=SUB)

        ring = ctx.enter_context(nc.psum_tensor("ring", [P, Y, CHUNK], F32))
        z_ps = ctx.enter_context(nc.psum_tensor("z_ps", [P, CHUNK], F32))

        consts_loaded = sem("consts_loaded")
        first_idx_loaded = sem("first_idx_loaded")
        raw_loaded = [sem(f"raw_loaded{i}") for i in range(RAW)]
        dense_loaded = sem("dense_loaded")
        W2_loaded = sem("W2_loaded")
        ident_zero = sem("ident_zero")
        idx_loaded = sem("idx_loaded")
        gathered = [sem(f"gathered{i}") for i in range(STAGE)]
        lo_ready = sem("lo_ready")
        pool_waited = sem("pool_waited")
        item_ready = sem("item_ready")
        quad_summed = sem("quad_summed")
        mlp_ready = sem("mlp_ready")
        hi_ready = sem("hi_ready")
        duo_saved = sem("duo_saved")
        cols_hi = sem("cols_hi")
        z_saved = sem("z_saved")
        mlp_used = sem("mlp_used")
        stored = sem("stored")
        sel_zero = sem("sel_zero")
        lo_ready_dve = sem("lo_ready_dve")
        tile_done = sem("tile_done")
        cols_ready = sem("cols_ready")
        consts_made = sem("consts_made")

        block = ctx.enter_context(nc.Block())

        item_at = {x: i for i, x in enumerate(ITEMS)}


        def items_to(c, kind, n):
            return c * NI + (item_at[kind, n] + 1 if n >= 0 else 0) + 1

        def tiles_to(c, t):
            return c * NT + t + 2

        def quads_to(c, q):
            return c * NQ + max(q + 1, 0) + 1

        def cols_to(c, k, h):
            return c * (FIELDS - 1) + 2 * k + h

        def wait_low(engine, c, q):
            if 0 <= q < DVE_LOW:
                engine.wait_ge(lo_ready_dve, c * DVE_LOW + q + 1)
            else:
                engine.wait_ge(lo_ready, c * (NQ - DVE_LOW) + max(q - DVE_LOW + 1, 0) + 1)

        def mlp_to(c, step):
            return c * MLP + STEPS.index(step) + 2

        def low_part(engine, done, c, q):
            engine.wait_ge(hi_ready, quads_to(c, q))
            engine.wait_ge(item_ready, items_to(c, "tile", QUAD * (q - SPLIT) + QUAD - 1))
            engine.tensor_tensor(
                w_lo[:, q % SPLIT, :], raw[:, q % RAW, :], w_hi[:, q % SPLIT, :], ALU.subtract
            ).then_inc(done, 1)

        @block.sync
        def _(sp):
            sp.dma_start(idx[:], ids_t[0]).then_inc(first_idx_loaded, 16)
            sp.dma_start(b1[:], b1t).then_inc(consts_loaded, 16)
            sp.dma_start(b2[:], b2t).then_inc(consts_loaded, 16)
            sp.dma_start(W3[:], W3t).then_inc(consts_loaded, 16)
            sp.wait_ge(first_idx_loaded, 16)
            sp.dma_start(W1[:], W1g).then_inc(consts_loaded, 16)

            def load_weights(q):
                for h in range(2):
                    sp.dma_start(raw[E * h : E * h + E, q % RAW, :], param_q[q]).then_inc(raw_loaded[q % RAW], 16)

            load_weights(0)
            with sp.Fori(0, CHUNKS) as c:
                for q in range(1, NQ):
                    wait_low(sp, c, q - RAW)
                    load_weights(q)
                wait_low(sp, c, NQ - 1)
                load_weights(0)
                sp.wait_ge(quad_summed, quads_to(c, NQ - 1))
                sp.dma_start(W2, W2t).then_inc(W2_loaded, 16)
                sp.wait_ge(z_saved, (c + 1) * NG + 1)
                sp.dma_start(
                    z[DENSE_ROW : DENSE_ROW + DENSE, NG - 1, :], dense_t[:, bass.ds(c * CHUNK, CHUNK)]
                ).then_inc(dense_loaded, 16)

        @block.gpsimd
        def _(pool):
            pool.memset(ident[:], 0.0).then_inc(ident_zero, 1)
            pool.wait_ge(ident_zero, 1)
            pool.affine_select(
                out=ident[:], in_=ident[:], compare_op=ALU.not_equal, fill=1.0, base=0, pattern=[[-1, P]],
                channel_multiplier=1,
            ).then_inc(consts_made, 1)

            def gather(c, n):
                k, f, t = n // DUO_GATHERS, n // BT, n % BT
                if n % DUO_GATHERS == 0 and k >= EARLY:
                    pool.wait_ge(item_ready, items_to(c, "duo", k - STAGE))
                    pool.sem_inc(pool_waited, 1)
                pool.indirect_dma_start(
                    stage[:, k % STAGE, t, E * (f % 2) : E * (f % 2) + E], None, tables[f],
                    bass.IndirectOffsetOnAxis(ap=idx[:, f, t : t + 1], axis=0),
                ).then_inc(gathered[k % STAGE], 16)

            pool.sem_inc(lo_ready, 1)
            pool.wait_ge(first_idx_loaded, 16)
            pool.sem_inc(pool_waited, 1)
            for n in range(EARLY * DUO_GATHERS):
                gather(0, n)
            with pool.Fori(0, CHUNKS) as c:
                done = EARLY * DUO_GATHERS
                for q in range(DVE_LOW, NQ):
                    needed = DUO_GATHERS * duos_at(QUAD * q - 1)
                    allowed = DUO_GATHERS * min(duos_at(QUAD * (q - 1) - 1) + STAGE, DUOS)
                    upto = max(needed, min(allowed, done + GATHERS))
                    for n in range(done, needed):
                        gather(c, n)
                    low_part(pool, lo_ready, c, q)
                    for n in range(max(done, needed), upto):
                        gather(c, n)
                    done = max(done, upto)
                assert done == DUO_GATHERS * DUOS
                pool.wait_ge(item_ready, items_to(c, "duo", DUOS - 1))
                pool.sem_inc(pool_waited, 1)
                pool.dma_start(
                    idx[:], ids_t[bass.ds(c + 1, 1)].rearrange("a p f t -> (a p) f t")
                ).then_inc(idx_loaded, 16)
                pool.wait_ge(idx_loaded, (c + 1) * 16)
                pool.sem_inc(pool_waited, 1)
                for n in range(EARLY * DUO_GATHERS):
                    gather(c + 1, n)

        @block.scalar
        def _(act):
            def high_part(c, q):
                act.wait_ge(raw_loaded[q % RAW], 32 * (c * len(range(q % RAW, NQ, RAW)) + q // RAW + 1))
                act.wait_ge(item_ready, items_to(c, "tile", QUAD * (q - SPLIT) + QUAD - 1))
                act.activation(w_hi[:, q % SPLIT, :], raw[:, q % RAW, :], ACT.Copy).then_inc(hi_ready, 1)

            def save_duo(c, k):
                i = item_at["duo", k]
                act.wait_ge(item_ready, items_to(c, "duo", k))
                act.activation(emb_t[:, k, :], ring[:, i % Y, :], ACT.Copy).then_inc(duo_saved, 1)
                act.wait_ge(duo_saved, c * DUOS + k + 1)
                if k:
                    act.activation(cols[0:E, k % 2, 0, :], emb_t[0:E, k, :], ACT.Copy).then_inc(cols_hi, 1)
                act.activation(cols[E:P, k % 2, 1, :], emb_t[E:P, k, :], ACT.Copy).then_inc(cols_hi, 1)

            def save_z(c, g):
                act.wait_ge(quad_summed, quads_to(c, min(SLOTS * (g + 1), NQ) - 1))
                act.activation(z[:, g, :], z_ps[:, :], ACT.Copy).then_inc(z_saved, 1)

            act.sem_inc(hi_ready, 1)
            act.sem_inc(z_saved, 1)
            act.sem_inc(mlp_used, 1)
            act.sem_inc(stored, 1)
            high_part(0, 0)
            for k in range(EARLY):
                save_duo(0, k)
            with act.Fori(0, CHUNKS) as c:
                for q in range(NQ):
                    for ahead in range(1, AHEAD + 1) if q == 0 else [AHEAD]:
                        if q + ahead < NQ:
                            high_part(c, q + ahead)
                    if q >= 2 and (q - 2) % SLOTS == SLOTS - 1:
                        save_z(c, (q - 2) // SLOTS)
                    for t in range(QUAD * q, QUAD * q + QUAD):
                        if t in AFTER:
                            save_duo(c, AFTER[t])
                save_z(c, NG - 1)
                act.wait_ge(consts_loaded, 16 * 4)
                for n, (layer, s, m) in enumerate(STEPS):
                    if n == SUBS * (H1 // P):
                        for k in range(EARLY):
                            save_duo(c + 1, k)
                        high_part(c + 1, 0)
                    act.wait_ge(mlp_ready, c * MLP + n + 1)
                    if layer == "h1":
                        act.activation(
                            h1[:, s, m, :], ring[:, m // 2, SUB * (m % 2) : SUB * (m % 2) + SUB], ACT.Relu,
                            bias=b1[:, m : m + 1],
                        ).then_inc(mlp_used, 1)
                    elif layer == "h2":
                        act.activation(
                            h2[:, s, m, :], ring[:, 2, SUB * m : SUB * m + SUB], ACT.Relu, bias=b2[:, m : m + 1]
                        ).then_inc(mlp_used, 1)
                    else:
                        act.activation(y_out[:, s, :], z_ps[0:1, SUB * s : SUB * s + SUB], ACT.Copy).then_inc(
                            mlp_used, 1
                        )
                        act.wait_ge(mlp_used, mlp_to(c, ("y", s, 0)))
                        act.dma_start(out_v[bass.ds(c * SUBS + s, 1), :], y_out[:, s, :]).then_inc(stored, 16)
            act.wait_ge(stored, 16 * CHUNKS * SUBS + 1)

        @block.vector
        def _(dve):
            dve.memset(sel[:], 0.0).then_inc(sel_zero, 1)
            dve.wait_ge(sel_zero, 1)
            dve.memset(sel[0:E, 30:31], 1.0).then_inc(consts_made, 1)
            dve.memset(sel[E:P, 31:32], 1.0).then_inc(consts_made, 1)

            def low_cols(c, k, h):
                dve.wait_ge(cols_hi, cols_to(c, k, h))
                here, there = slice(E * h, E * h + E), slice(E - E * h, P - E * h)
                dve.tensor_tensor(
                    cols[there, k % 2, h, :], emb_t[here, k, :], cols[here, k % 2, h, :], ALU.subtract
                ).then_inc(cols_ready, 1)

            dve.sem_inc(tile_done, 1)
            for k, h in EARLY_COLS:
                low_cols(0, k, h)
            low_part(dve, lo_ready_dve, 0, 0)
            with dve.Fori(0, CHUNKS) as c:
                for t in range(NT):
                    dve.wait_ge(item_ready, items_to(c, "tile", t))
                    if t == PROD - 1:
                        dve.wait_ge(stored, 16 * SUBS * c + 1)
                    dve.wait_ge(quad_summed, quads_to(c, (t - PROD) // QUAD))
                    dve.tensor_tensor(
                        prod[:, t % PROD, :], ring[:, item_at["tile", t] % Y, :], emb_t[:, TILES[t][1], :], ALU.mult
                    ).then_inc(tile_done, 1)
                    if t % QUAD == LOW_AT and t // QUAD + 1 < DVE_LOW:
                        low_part(dve, lo_ready_dve, c, t // QUAD + 1)
                    for k, h in LOW_AFTER.get(t, ()):
                        low_cols(c, k, h)
                for k, h in EARLY_COLS:
                    low_cols(c + 1, k, h)
                low_part(dve, lo_ready_dve, c + 1, 0)

        @block.tensor
        def _(pe):
            pe.wait_ge(consts_made, 3)

            def slot_free(c, i):
                if i >= Y:
                    kind, n = ITEMS[i - Y]
                    if kind == "duo":
                        pe.wait_ge(duo_saved, c * DUOS + n + 1)
                    else:
                        pe.wait_ge(tile_done, tiles_to(c, n))

            def transpose_duo(c, k):
                i = item_at["duo", k]
                pe.wait_ge(gathered[k % STAGE], 16 * DUO_GATHERS * (c * (DUOS // STAGE) + k // STAGE + 1))
                slot_free(c, i)
                for t in range(BT):
                    mm = pe.transpose(ring[:, i % Y, P * t : P * t + P], stage[:, k % STAGE, t, :], ident[:])
                mm.then_inc(item_ready, 1)

            def multiply(c, t):
                i = item_at["tile", t]
                col, _ = TILES[t]
                q, j = divmod(t, QUAD)
                if t in FIRST:
                    pe.wait_ge(cols_ready, cols_to(c, *FIRST[t]))
                if j == 0:
                    wait_low(pe, c, q)
                slot_free(c, i)
                for w in (w_lo, w_hi):
                    for s in range(SUBS):
                        mm = pe.matmul(
                            ring[:, i % Y, SUB * s : SUB * s + SUB], w[:, q % SPLIT, P * j : P * j + P],
                            cols[:, col // 2 % 2, col % 2, SUB * s : SUB * s + SUB],
                            start=(w is w_lo), stop=(w is w_hi),
                        )
                mm.then_inc(item_ready, 1)

            def sum_products(c, q):
                pe.wait_ge(tile_done, tiles_to(c, QUAD * q + QUAD - 1))
                g, slot = divmod(q, SLOTS)
                if slot == 0:
                    pe.wait_ge(z_saved, c * NG + g + 1)
                    if g == 0:
                        pe.wait_ge(mlp_used, c * MLP + 1)
                last = slot == SLOTS - 1 or q == NQ - 1
                for s in range(SUBS):
                    for j in range(QUAD):
                        mm = pe.matmul(
                            z_ps[32 * j : 32 * j + 32, SUB * s : SUB * s + SUB], sel[:, 30 - 2 * slot : 62 - 2 * slot],
                            prod[:, (QUAD * q + j) % PROD, SUB * s : SUB * s + SUB], start=(slot == 0), stop=last,
                        )
                mm.then_inc(quad_summed, 1)

            def h1_part(c, n, groups):
                _, s, m = STEPS[n]
                for g in groups:
                    mm = pe.matmul(
                        ring[:, m // 2, SUB * (m % 2) : SUB * (m % 2) + SUB], W1[:, g, P * m : P * m + P],
                        z[:, g, SUB * s : SUB * s + SUB], start=(g == 0), stop=(g == NG - 1),
                    )
                if NG - 1 in groups:
                    mm.then_inc(mlp_ready, 1)

            def mlp_start(c):
                assert STEPS[:2] == [("h1", 0, 0), ("h1", 0, 1)]
                pe.wait_ge(consts_loaded, 16 * 4)
                pe.wait_ge(z_saved, c * NG + NG)
                slot_free(c, NI)
                h1_part(c, 0, range(NG - 1))
                sum_products(c, NQ - 1)
                h1_part(c, 1, range(NG - 1))
                pe.wait_ge(z_saved, (c + 1) * NG + 1)
                pe.wait_ge(dense_loaded, (c + 1) * 16)
                h1_part(c, 0, [NG - 1])
                h1_part(c, 1, [NG - 1])

            def mlp_rest(c):
                for n, (layer, s, m) in enumerate(STEPS):
                    if n < 2:
                        continue
                    if layer == "h1":
                        if s:
                            pe.wait_ge(mlp_used, mlp_to(c, ("h1", s - 1, m)))
                        h1_part(c, n, range(NG))
                        continue
                    if layer == "h2":
                        if (s, m) == (0, 0):
                            pe.wait_ge(W2_loaded, (c + 1) * 16)
                            for k in range(EARLY):
                                pe.wait_ge(mlp_used, mlp_to(c, ("h1", SUBS - 1, 2 * k + 1)))
                                transpose_duo(c + 1, k)
                        before = ("h2", s - 1, m) if s else ("h1", s, H1 // P - 1)
                        pe.wait_ge(mlp_used, mlp_to(c, before))
                        for g in range(H1 // P):
                            mm = pe.matmul(
                                ring[:, 2, SUB * m : SUB * m + SUB], W2[:, g, P * m : P * m + P], h1[:, s, g, :],
                                start=(g == 0), stop=(g == H1 // P - 1),
                            )
                    else:
                        pe.wait_ge(mlp_used, mlp_to(c, ("h2", s, H2 // P - 1)))
                        for g in range(H2 // P):
                            mm = pe.matmul(
                                z_ps[0:1, SUB * s : SUB * s + SUB], W3[:, g : g + 1], h2[:, s, g, :],
                                start=(g == 0), stop=(g == H2 // P - 1),
                            )
                    mm.then_inc(mlp_ready, 1)

            pe.sem_inc(item_ready, 1)
            pe.sem_inc(quad_summed, 1)
            for k in range(EARLY):
                transpose_duo(0, k)
            with pe.Fori(0, CHUNKS) as c:
                for q in range(NQ):
                    for t in range(QUAD * q, QUAD * q + QUAD):
                        multiply(c, t)
                        if t in AFTER:
                            transpose_duo(c, AFTER[t])
                    if q:
                        sum_products(c, q - 1)
                mlp_start(c)
                mlp_rest(c)


def kernel(**inputs):
    import concourse.bacc as bacc
    from concourse.bass_utils import run_bass_kernel_spmd

    nc = bacc.Bacc("TRN2", target_bir_lowering=False, num_devices=1)
    W = {k: np.asarray(v) for k, v in inputs.items()}

    param = W["L0_rec_param"]
    param_q = np.zeros((NQ, E, QUAD, 2, E), param.dtype)
    W1g = np.zeros((P, NG, H1), W["W_top1"].dtype)
    for t, (c, k) in enumerate(TILES):
        q, j = divmod(t, QUAD)
        g, slot = divmod(q, SLOTS)
        for h in range(2):
            r = 2 * k + h
            if r < c:
                param_q[q, :, j, h] = param[:, pair_index(r, c)]
                W1g[32 * j + 2 * slot + h, g] = W["W_top1"][pair_index(r, c)]
    W1g[DENSE_ROW : DENSE_ROW + DENSE, NG - 1] = W["W_top1"][-DENSE:]

    ids_t = W["ids"].reshape(CHUNKS, BT, P, FIELDS).transpose(0, 2, 3, 1)
    arrays = {
        "dense_t": np.ascontiguousarray(W["dense_ctx"].T),
        "ids_t": np.concatenate([ids_t, ids_t[:1]]),
        "param_q": param_q.reshape(NQ, E, QUAD * P),
        "W1g": W1g,
        "b1t": np.ascontiguousarray(W["b_top1"].reshape(H1 // P, P).T),
        "W2t": np.ascontiguousarray(W["W_top2"].reshape(H1 // P, P, H2).transpose(1, 0, 2)),
        "b2t": np.ascontiguousarray(W["b_top2"].reshape(H2 // P, P).T),
        "W3t": np.ascontiguousarray(W["W_top3"].reshape(H2 // P, P).T),
    }
    for f in range(FIELDS):
        arrays[f"tbl_{f}"] = np.ascontiguousarray(W[f"tbl_{f}"])
    ap = {
        name: nc.dram_tensor(name, a.shape, mybir.dt.from_np(a.dtype), kind="ExternalInput").ap()
        for name, a in arrays.items()
    }
    out = nc.dram_tensor("out", (B, 1), F32, kind="ExternalOutput").ap()
    tables = [ap[f"tbl_{f}"] for f in range(FIELDS)]
    fm_mlp_kernel(
        nc, ap["dense_t"], ap["ids_t"], tables, ap["param_q"], ap["W1g"], ap["b1t"], ap["W2t"], ap["b2t"], ap["W3t"],
        out,
    )
    r = run_bass_kernel_spmd(nc, [arrays], core_ids=[0])
    return r.results[0]["out"]
```
